# Optimizing a Trainium2 kernel written in Bass

```python
import numpy as np
import jax
import jax.numpy as jnp

def _softmax(x, axis=-1):
    return jax.nn.softmax(x, axis=axis)

def _gelu(x):
    return jax.nn.gelu(x, approximate=True)

def _silu(x):
    return jax.nn.silu(x)

def _sigmoid(x):
    return jax.nn.sigmoid(x)

def _layernorm(x, axis=-1, eps=1e-05):
    m = jnp.mean(x, axis=axis, keepdims=True)
    v = jnp.var(x, axis=axis, keepdims=True)
    return (x - m) / jnp.sqrt(v + eps)

def _scatter_add(tgt, idx, src, axis=0):
    return tgt.at[idx].add(src)

def _segment_sum(src, seg, n):
    return jax.ops.segment_sum(src, seg, n)
kernel_name = 'mk_gnn_preln_d4_gnn_r16_bafd2a'

def setup_inputs(seed: int=0):
    np.random.seed(seed)
    _w = jnp.asarray

    def _rec_inputs():
        import jax
        import jax.numpy as jnp
        _gk = jax.random.key(seed)
        x = -0.000202 + 1 * jax.random.normal(jax.random.fold_in(_gk, 1), (6250, 64), jnp.float32)
        src = jax.random.randint(jax.random.fold_in(_gk, 2), (200000,), 0, 6250, jnp.int32)
        dst = jax.random.randint(jax.random.fold_in(_gk, 3), (200000,), 0, 6250, jnp.int32)
        _o = jnp.argsort(dst, stable=True)
        src = src[_o]
        dst = dst[_o]
        edge_attr_64 = -5.16925e-05 + 1.00005 * jax.random.normal(jax.random.fold_in(_gk, 12), (200000, 64), jnp.float32)
        return (x, src, dst, edge_attr_64)
    x, src, dst, edge_attr_64 = _rec_inputs()

    def _L0_gnn_setup():
        import jax, jax.numpy as jnp
        import numpy as np
        N = 6250
        E = 100000
        D = 64
        NEG_SLOPE = 0.2
        EPS_IN = 1e-05

        def _instance_norm(h):
            mu = h.mean(-1, keepdims=True)
            var = ((h - mu) ** 2).mean(-1, keepdims=True)
            return (h - mu) * jax.lax.rsqrt(var + EPS_IN)

        def _gatv2(x, src, dst, edge_attr, Wl, bl, Wr, br, We, att, bo):
            xl = x @ Wl.T + bl
            xr = x @ Wr.T + br
            e = edge_attr @ We.T
            m = xl[src] + xr[dst] + e
            score = jnp.where(m > 0, m, NEG_SLOPE * m) @ att
            smax = jax.ops.segment_max(score, dst, num_segments=N)
            smax = jnp.where(jnp.isfinite(smax), smax, 0.0)
            es = jnp.exp(score - smax[dst])
            denom = jax.ops.segment_sum(es, dst, num_segments=N)
            alpha = es / (denom[dst] + 1e-16)
            out = jax.ops.segment_sum(alpha[:, None] * xl[src], dst, num_segments=N)
            return out + bo
        key = jax.random.key(seed)
        ks = jax.random.split(key, 24)
        s = 0.05
        p = lambda k, shape: jax.random.normal(k, shape, jnp.float32) * s
        inp = {'x': jax.random.normal(ks[0], (N, D), jnp.float32), 'edge_index': jax.random.randint(ks[1], (2, E), 0, N, dtype=jnp.int64), 'edge_attr': jax.random.normal(ks[2], (E, D), jnp.float32), 'Wl1': p(ks[3], (D, D)), 'bl1': p(ks[4], (D,)), 'Wr1': p(ks[5], (D, D)), 'br1': p(ks[6], (D,)), 'We1': p(ks[7], (D, D)), 'att1': p(ks[8], (D,)), 'bo1': p(ks[9], (D,)), 'Wl2': p(ks[10], (D, D)), 'bl2': p(ks[11], (D,)), 'Wr2': p(ks[12], (D, D)), 'br2': p(ks[13], (D,)), 'We2': p(ks[14], (D, D)), 'att2': p(ks[15], (D,)), 'bo2': p(ks[16], (D,)), 'Wskip': p(ks[17], (D, D)), 'bskip': p(ks[18], (D,))}
        return inp
    _L0_gnn_all = _L0_gnn_setup()
    _L0_gnn_in = {k: v for k, v in _L0_gnn_all.items() if k in ('Wl1', 'bl1', 'Wr1', 'br1', 'We1', 'att1', 'bo1', 'Wl2', 'bl2', 'Wr2', 'br2', 'We2', 'att2', 'bo2', 'Wskip', 'bskip')}
    del _L0_gnn_all

    def _L1_gnn_setup():
        import jax, jax.numpy as jnp
        import numpy as np
        N_NODES = 6250
        N_EDGES = 100000
        D = 64
        BN_EPS = 1e-05
        key = jax.random.key(seed)
        ks = jax.random.split(key, 10)
        s = 1.0 / np.sqrt(D)
        return {'features': jax.random.normal(ks[0], (N_NODES, D), dtype=jnp.float32), 'src': jax.random.randint(ks[1], (N_EDGES,), 0, N_NODES, dtype=jnp.int32), 'dst': jax.random.randint(ks[2], (N_EDGES,), 0, N_NODES, dtype=jnp.int32), 'eps': jnp.zeros((), dtype=jnp.float32), 'W1': jax.random.uniform(ks[3], (D, D), jnp.float32, -s, s), 'b1': jax.random.uniform(ks[4], (D,), jnp.float32, -s, s), 'W2': jax.random.uniform(ks[5], (D, D), jnp.float32, -s, s), 'b2': jax.random.uniform(ks[6], (D,), jnp.float32, -s, s), 'gamma': jnp.ones((D,), dtype=jnp.float32), 'beta': jnp.zeros((D,), dtype=jnp.float32)}
    _L1_gnn_all = _L1_gnn_setup()
    _L1_gnn_in = {k: v for k, v in _L1_gnn_all.items() if k in ('eps', 'W1', 'b1', 'W2', 'b2', 'gamma', 'beta')}
    del _L1_gnn_all

    def _L2_gnn_setup():
        import jax, jax.numpy as jnp
        import numpy as np
        import math
        N_NODES = 6250
        D = 64
        N_EDGES = 80000
        LN_EPS = 1e-05
        key = jax.random.key(seed)
        ks = jax.random.split(key, 8)
        x = jax.random.normal(ks[0], (N_NODES, D), dtype=jnp.float32)
        edge_index = jax.random.randint(ks[1], (2, N_EDGES), 0, N_NODES, dtype=jnp.int64)
        limit = 0.1 * math.sqrt(6.0 / (D + D))
        qk_w = jax.random.uniform(ks[2], (D, D), dtype=jnp.float32, minval=-limit, maxval=limit)
        v_w = jax.random.uniform(ks[3], (D, D), dtype=jnp.float32, minval=-limit, maxval=limit)
        o_w = jax.random.uniform(ks[4], (D, D), dtype=jnp.float32, minval=-limit, maxval=limit)
        qk_b = jnp.zeros((D,), dtype=jnp.float32)
        v_b = jnp.zeros((D,), dtype=jnp.float32)
        o_b = jnp.zeros((D,), dtype=jnp.float32)
        ln_g = jnp.ones((D,), dtype=jnp.float32)
        ln_b = jnp.zeros((D,), dtype=jnp.float32)
        return {'x': x, 'edge_index': edge_index, 'qk_w': qk_w, 'qk_b': qk_b, 'v_w': v_w, 'v_b': v_b, 'o_w': o_w, 'o_b': o_b, 'ln_g': ln_g, 'ln_b': ln_b}
    _L2_gnn_all = _L2_gnn_setup()
    _L2_gnn_in = {k: v for k, v in _L2_gnn_all.items() if k in ('qk_w', 'qk_b', 'v_w', 'v_b', 'o_w', 'o_b', 'ln_g', 'ln_b')}
    del _L2_gnn_all

    def _L3_gnn_setup():
        import jax, jax.numpy as jnp
        import numpy as np
        N_NODES = 3125
        N_EDGES = 50000
        IN_DIM, HID_DIM, OUT_DIM = (64, 128, 64)

        def gcn_conv(x, src, dst, W, b, n_nodes):
            h = x @ W
            ones = jnp.ones(src.shape[0], dtype=x.dtype)
            deg = jax.ops.segment_sum(ones, dst, num_segments=n_nodes)
            dinv = jnp.where(deg > 0, jax.lax.rsqrt(deg), 0.0).astype(x.dtype)
            norm = dinv[src] * dinv[dst]
            msg = h[src] * norm[:, None]
            out = jax.ops.segment_sum(msg, dst, num_segments=n_nodes)
            return out + b
        key = jax.random.key(seed)
        k1, k2, k3, k4 = jax.random.split(key, 4)
        z = jax.random.normal(k1, (N_NODES, IN_DIM), dtype=jnp.float32)
        edge_index = jax.random.randint(k2, (2, N_EDGES), 0, N_NODES, dtype=jnp.int64)
        W1 = jax.random.normal(k3, (IN_DIM, HID_DIM), dtype=jnp.float32) / np.sqrt(IN_DIM)
        b1 = jnp.zeros((HID_DIM,), dtype=jnp.float32)
        W2 = jax.random.normal(k4, (HID_DIM, OUT_DIM), dtype=jnp.float32) / np.sqrt(HID_DIM)
        b2 = jnp.zeros((OUT_DIM,), dtype=jnp.float32)
        return {'z': z, 'edge_index': edge_index, 'W1': W1, 'b1': b1, 'W2': W2, 'b2': b2}
    _L3_gnn_all = _L3_gnn_setup()
    _L3_gnn_in = {k: v for k, v in _L3_gnn_all.items() if k in ('W1', 'b1', 'W2', 'b2')}
    del _L3_gnn_all
    return {'x': x, 'src': src, 'dst': dst, 'edge_attr_64': edge_attr_64, 'L0_gnn_Wl1': _L0_gnn_in['Wl1'], 'L0_gnn_bl1': _L0_gnn_in['bl1'], 'L0_gnn_Wr1': _L0_gnn_in['Wr1'], 'L0_gnn_br1': _L0_gnn_in['br1'], 'L0_gnn_We1': _L0_gnn_in['We1'], 'L0_gnn_att1': _L0_gnn_in['att1'], 'L0_gnn_bo1': _L0_gnn_in['bo1'], 'L0_gnn_Wl2': _L0_gnn_in['Wl2'], 'L0_gnn_bl2': _L0_gnn_in['bl2'], 'L0_gnn_Wr2': _L0_gnn_in['Wr2'], 'L0_gnn_br2': _L0_gnn_in['br2'], 'L0_gnn_We2': _L0_gnn_in['We2'], 'L0_gnn_att2': _L0_gnn_in['att2'], 'L0_gnn_bo2': _L0_gnn_in['bo2'], 'L0_gnn_Wskip': _L0_gnn_in['Wskip'], 'L0_gnn_bskip': _L0_gnn_in['bskip'], 'L1_gnn_eps': _L1_gnn_in['eps'], 'L1_gnn_W1': _L1_gnn_in['W1'], 'L1_gnn_b1': _L1_gnn_in['b1'], 'L1_gnn_W2': _L1_gnn_in['W2'], 'L1_gnn_b2': _L1_gnn_in['b2'], 'L1_gnn_gamma': _L1_gnn_in['gamma'], 'L1_gnn_beta': _L1_gnn_in['beta'], 'L2_gnn_qk_w': _L2_gnn_in['qk_w'], 'L2_gnn_qk_b': _L2_gnn_in['qk_b'], 'L2_gnn_v_w': _L2_gnn_in['v_w'], 'L2_gnn_v_b': _L2_gnn_in['v_b'], 'L2_gnn_o_w': _L2_gnn_in['o_w'], 'L2_gnn_o_b': _L2_gnn_in['o_b'], 'L2_gnn_ln_g': _L2_gnn_in['ln_g'], 'L2_gnn_ln_b': _L2_gnn_in['ln_b'], 'L3_gnn_W1': _L3_gnn_in['W1'], 'L3_gnn_b1': _L3_gnn_in['b1'], 'L3_gnn_W2': _L3_gnn_in['W2'], 'L3_gnn_b2': _L3_gnn_in['b2']}

def reference(x, src, dst, edge_attr_64, L0_gnn_Wl1, L0_gnn_bl1, L0_gnn_Wr1, L0_gnn_br1, L0_gnn_We1, L0_gnn_att1, L0_gnn_bo1, L0_gnn_Wl2, L0_gnn_bl2, L0_gnn_Wr2, L0_gnn_br2, L0_gnn_We2, L0_gnn_att2, L0_gnn_bo2, L0_gnn_Wskip, L0_gnn_bskip, L1_gnn_eps, L1_gnn_W1, L1_gnn_b1, L1_gnn_W2, L1_gnn_b2, L1_gnn_gamma, L1_gnn_beta, L2_gnn_qk_w, L2_gnn_qk_b, L2_gnn_v_w, L2_gnn_v_b, L2_gnn_o_w, L2_gnn_o_b, L2_gnn_ln_g, L2_gnn_ln_b, L3_gnn_W1, L3_gnn_b1, L3_gnn_W2, L3_gnn_b2):
    import jax
    import jax.numpy as jnp

    def _L0_gnn_ref(x, edge_index, edge_attr, Wl1, bl1, Wr1, br1, We1, att1, bo1, Wl2, bl2, Wr2, br2, We2, att2, bo2, Wskip, bskip):
        import jax, jax.numpy as jnp
        import numpy as np
        N = 6250
        E = 100000
        D = 64
        NEG_SLOPE = 0.2
        EPS_IN = 1e-05

        def _instance_norm(h):
            mu = h.mean(-1, keepdims=True)
            var = ((h - mu) ** 2).mean(-1, keepdims=True)
            return (h - mu) * jax.lax.rsqrt(var + EPS_IN)

        def _gatv2(x, src, dst, edge_attr, Wl, bl, Wr, br, We, att, bo):
            xl = x @ Wl.T + bl
            xr = x @ Wr.T + br
            e = edge_attr @ We.T
            m = xl[src] + xr[dst] + e
            score = jnp.where(m > 0, m, NEG_SLOPE * m) @ att
            smax = jax.ops.segment_max(score, dst, num_segments=N)
            smax = jnp.where(jnp.isfinite(smax), smax, 0.0)
            es = jnp.exp(score - smax[dst])
            denom = jax.ops.segment_sum(es, dst, num_segments=N)
            alpha = es / (denom[dst] + 1e-16)
            out = jax.ops.segment_sum(alpha[:, None] * xl[src], dst, num_segments=N)
            return out + bo
        src, dst = (edge_index[0], edge_index[1])
        h = jax.nn.relu(_gatv2(x, src, dst, edge_attr, Wl1, bl1, Wr1, br1, We1, att1, bo1))
        h = _instance_norm(h)
        h2 = jax.nn.relu(_gatv2(h, src, dst, edge_attr, Wl2, bl2, Wr2, br2, We2, att2, bo2) + x @ Wskip.T + bskip)
        return _instance_norm(h2)

    def _L1_gnn_ref(features, src, dst, eps, W1, b1, W2, b2, gamma, beta):
        import jax, jax.numpy as jnp
        import numpy as np
        N_NODES = 6250
        N_EDGES = 100000
        D = 64
        BN_EPS = 1e-05
        h_in = features
        neigh = jax.ops.segment_sum(features[src], dst, num_segments=N_NODES)
        h = (1.0 + eps) * features + neigh
        h = jnp.maximum(h @ W1 + b1, 0.0) @ W2 + b2
        mean = jnp.mean(h, axis=0)
        var = jnp.var(h, axis=0)
        h = (h - mean) * jax.lax.rsqrt(var + BN_EPS) * gamma + beta
        h = jnp.maximum(h, 0.0)
        h = h_in + h
        return h

    def _L2_gnn_ref(x, edge_index, qk_w, qk_b, v_w, v_b, o_w, o_b, ln_g, ln_b):
        import jax, jax.numpy as jnp
        import numpy as np
        import math
        N_NODES = 6250
        D = 64
        N_EDGES = 80000
        LN_EPS = 1e-05
        n = x.shape[0]
        qk = x @ qk_w.T + qk_b
        v = x @ v_w.T + v_b
        src = edge_index[0]
        dst = edge_index[1]
        scores = jnp.sum(qk[dst] * qk[src], axis=-1) / math.sqrt(v.shape[-1])
        scores = jnp.clip(scores, -5.0, 5.0)
        seg_max = jax.ops.segment_max(scores, dst, num_segments=n)
        e = jnp.exp(scores - seg_max[dst])
        seg_sum = jax.ops.segment_sum(e, dst, num_segments=n)
        attn = e / seg_sum[dst]
        out = jax.ops.segment_sum(attn[:, None] * v[src], dst, num_segments=n)
        out = out @ o_w.T + o_b
        h = out + x
        mu = jnp.mean(h, axis=-1, keepdims=True)
        var = jnp.mean(jnp.square(h - mu), axis=-1, keepdims=True)
        h = (h - mu) * jax.lax.rsqrt(var + LN_EPS)
        return h * ln_g + ln_b

    def _L3_gnn_ref(z, edge_index, W1, b1, W2, b2):
        import jax, jax.numpy as jnp
        import numpy as np
        N_NODES = 3125
        N_EDGES = 50000
        IN_DIM, HID_DIM, OUT_DIM = (64, 128, 64)

        def gcn_conv(x, src, dst, W, b, n_nodes):
            h = x @ W
            ones = jnp.ones(src.shape[0], dtype=x.dtype)
            deg = jax.ops.segment_sum(ones, dst, num_segments=n_nodes)
            dinv = jnp.where(deg > 0, jax.lax.rsqrt(deg), 0.0).astype(x.dtype)
            norm = dinv[src] * dinv[dst]
            msg = h[src] * norm[:, None]
            out = jax.ops.segment_sum(msg, dst, num_segments=n_nodes)
            return out + b
        n = z.shape[0]
        loops = jnp.arange(n, dtype=edge_index.dtype)
        src = jnp.concatenate([edge_index[0], loops])
        dst = jnp.concatenate([edge_index[1], loops])
        h = jax.nn.relu(gcn_conv(z, src, dst, W1, b1, n))
        x_hat = gcn_conv(h, src, dst, W2, b2, n)
        return x_hat
    edge_index = jnp.stack([src, dst])
    h = jnp.maximum(_layernorm(x, axis=-1), 0.0)
    x = x + _L0_gnn_ref(h, edge_index, edge_attr_64, L0_gnn_Wl1, L0_gnn_bl1, L0_gnn_Wr1, L0_gnn_br1, L0_gnn_We1, L0_gnn_att1, L0_gnn_bo1, L0_gnn_Wl2, L0_gnn_bl2, L0_gnn_Wr2, L0_gnn_br2, L0_gnn_We2, L0_gnn_att2, L0_gnn_bo2, L0_gnn_Wskip, L0_gnn_bskip)
    h = jnp.maximum(_layernorm(x, axis=-1), 0.0)
    x = x + _L1_gnn_ref(h, src, dst, L1_gnn_eps, L1_gnn_W1, L1_gnn_b1, L1_gnn_W2, L1_gnn_b2, L1_gnn_gamma, L1_gnn_beta)
    h = jnp.maximum(_layernorm(x, axis=-1), 0.0)
    x = x + _L2_gnn_ref(h, edge_index, L2_gnn_qk_w, L2_gnn_qk_b, L2_gnn_v_w, L2_gnn_v_b, L2_gnn_o_w, L2_gnn_o_b, L2_gnn_ln_g, L2_gnn_ln_b)
    h = jnp.maximum(_layernorm(x, axis=-1), 0.0)
    x = x + _L3_gnn_ref(h, edge_index, L3_gnn_W1, L3_gnn_b1, L3_gnn_W2, L3_gnn_b2)
    return x

_drawn_inputs = setup_inputs


def setup_inputs(seed=0):
    import zlib

    import numpy as np

    out = dict(_drawn_inputs(seed))
    spreads = {'L1_gnn_gamma': (1.0, 0.2),
     'L1_gnn_beta': (0.0, 0.1),
     'L2_gnn_qk_b': (0.0, 0.8),
     'L2_gnn_v_b': (0.0, 0.8),
     'L2_gnn_o_b': (0.0, 0.1),
     'L2_gnn_ln_g': (1.0, 0.2),
     'L2_gnn_ln_b': (0.0, 0.1),
     'L3_gnn_b1': (0.0, 0.357),
     'L3_gnn_b2': (0.0, 0.267)}
    factors = {'edge_attr_64': 8.0,
     'L0_gnn_Wr1': 8.0,
     'L0_gnn_br1': 8.0,
     'L0_gnn_We1': 8.0,
     'L0_gnn_att1': 5.266,
     'L0_gnn_Wr2': 8.0,
     'L0_gnn_br2': 8.0,
     'L0_gnn_We2': 8.0,
     'L0_gnn_att2': 8.0,
     'L1_gnn_b1': 8.0,
     'L1_gnn_b2': 8.0,
     'L2_gnn_qk_w': 8.0,
     'L2_gnn_v_w': 8.0,
     'L2_gnn_o_w': 8.0}
    for name, (base, spread) in spreads.items():
        noise = np.random.default_rng([zlib.crc32(name.encode()), seed]).standard_normal(out[name].shape)
        drawn = base * np.exp(spread * noise) if base else spread * noise
        out[name] = jnp.asarray(drawn.astype(out[name].dtype))
    for name, factor in factors.items():
        out[name] = (out[name] * factor).astype(out[name].dtype)
    return out
```

```python
import concourse.bass as bass
from concourse import mybir
from contextlib import ExitStack
import numpy as np

F32 = mybir.dt.float32
BF16 = mybir.dt.bfloat16
I32 = mybir.dt.int32
I16 = mybir.dt.int16
ALU = mybir.AluOpType
ACT = mybir.ActivationFunctionType
AX = mybir.AxisListType

P = 128
N = 6250
D = 64
E = 200000
NT = -(-N // P)
NP = NT * P
GE = 512
GC = GE // P
NG = -(-E // GE)
EP = NG * GE
NGC = -(-NG // P)
NGP = NGC * P
TB = 7
RING = 8
DRAIN = 5
LEAD = 8
VCOLS = -(-(NG * NT + 2 * RING + DRAIN) // P)
VTAB = VCOLS * P
IDLE = NT
CT = 4
NQ = EP // (CT * P)
WD = 32
WB = 8
PACK = 1024
NW = NP // WD
NWC = -(-NW // P)
NWP = NWC * P
NCC = -(-CT * NQ // P)
CODE = 64
FREE = 16
ROW = D + 2 + 3 * D // 2
MASK = -1.0e30
FLOOR = -1.0e29
EPS = 1.0e-5


class Kit:

    def __init__(self, nc, ctx):
        self.nc, self.ctx = nc, ctx

    def sb(self, name, shape, dt=F32, ctx=None):
        return (ctx or self.ctx).enter_context(self.nc.sbuf_tensor(name, shape, dt))

    def ps(self, name, shape, dt=F32, ctx=None):
        return (ctx or self.ctx).enter_context(self.nc.psum_tensor(name, shape, dt))

    def sem(self, name):
        self.sems.append(self.held.enter_context(self.nc.semaphore(name)))
        return self.sems[-1]


def phase(build_phase):
    def phased(nc, k, *args, **kw):
        k.held, k.sems = ExitStack(), []
        build_phase(nc, k, *args, **kw)
        with nc.Block() as block:
            @block.gpsimd
            def _(pool):
                for sem in k.sems:
                    pool.sem_clear(sem)
        k.held.close()
    return phased


def per_node(stat):
    return stat[:, 0:NT].unsqueeze(2).to_broadcast([P, NT, D])


@phase
def load_nodes(nc, k, x_d, x_sb, ident, identb, iota_node, ones):
    s_x, s_z, s_pool = k.sem("x_loaded"), k.sem("x_zeroed"), k.sem("const_made")
    full = N // P
    with nc.Block() as block:
        @block.vector
        def _(dve):
            dve.memset(x_sb[:], 0.0).then_inc(s_z, 1)
            dve.memset(ones[:], 1.0)

        @block.sync
        def _(sp):
            sp.wait_ge(s_z, 1)
            sp.dma_start(x_sb[:, 0:full, :], x_d[0:full * P, :].rearrange("(t p) f -> p t f", p=P)).then_inc(s_x, 16)
            sp.dma_start(x_sb[0:N - full * P, full, :], x_d[full * P:N, :]).then_inc(s_x, 16)
            sp.wait_ge(s_x, 32)

        @block.gpsimd
        def _(pool):
            pool.memset(ident[:], 0.0).then_inc(s_pool, 1)
            pool.wait_ge(s_pool, 1)
            pool.affine_select(out=ident[:], in_=ident[:], compare_op=ALU.not_equal, fill=1.0, base=0,
                               pattern=[[-1, P]], channel_multiplier=1).then_inc(s_pool, 1)
            pool.wait_ge(s_pool, 2)
            pool.tensor_copy(identb[:], ident[:])
            pool.iota(iota_node[:], [[P, NT + 1]], base=0, channel_multiplier=1,
                      allow_small_or_imprecise_dtypes=True)


@phase
def layer_norm(nc, k, tag, src, dst, tmp, st, relu_in=False, relu_out=False, add_to=None):
    s_var, s_sd = k.sem(tag + "_var"), k.sem(tag + "_sd")
    mean, var, sd, rs = (st[:, j, :] for j in range(4))
    with nc.Block() as block:
        @block.vector
        def _(dve):
            if relu_in:
                dve.tensor_scalar(src[:], src[:], 0.0, None, ALU.max)
                dve.drain()
            dve.tensor_reduce(mean[:, 0:NT], src[:], AX.X, ALU.add)
            dve.drain()
            dve.tensor_scalar(mean[:, 0:NT], mean[:, 0:NT], 1.0 / D, None, ALU.mult)
            dve.drain()
            dve.tensor_tensor(dst[:], src[:], per_node(mean), ALU.subtract)
            dve.drain()
            dve.tensor_tensor(tmp[:], dst[:], dst[:], ALU.mult)
            dve.drain()
            dve.tensor_reduce(var[:, 0:NT], tmp[:], AX.X, ALU.add)
            dve.drain()
            dve.tensor_scalar(var[:, 0:NT], var[:, 0:NT], 1.0 / D, EPS, ALU.mult, ALU.add).then_inc(s_var, 1)
            dve.wait_ge(s_sd, 1)
            dve.reciprocal(rs[:, 0:NT], sd[:, 0:NT])
            dve.drain()
            dve.tensor_tensor(dst[:], dst[:], per_node(rs), ALU.mult)
            dve.drain()
            if relu_out:
                dve.tensor_scalar(dst[:], dst[:], 0.0, None, ALU.max)
                dve.drain()
            if add_to is not None:
                dve.tensor_tensor(add_to[:], add_to[:], dst[:], ALU.add)
                dve.drain()

        @block.scalar
        def _(act):
            act.wait_ge(s_var, 1)
            act.activation(sd[:, 0:NT], var[:, 0:NT], ACT.Sqrt).then_inc(s_sd, 1)


@phase
def linear(nc, k, tag, h, w_d, width, out, ident):
    s_w, s_one = k.sem(tag + "_w"), k.sem(tag + "_one")
    s_stage, s_tr, s_ht, s_mm = (k.sem(tag + x) for x in ("_staged", "_turned", "_ht", "_mm"))
    s_out = k.sem(tag + "_out")
    with ExitStack() as own:
        w_sb = k.sb(tag + "_w_sb", [D + 1, width], F32, own)
        stage = k.sb(tag + "_stage", [P, TB, D], F32, own)
        ht = k.sb(tag + "_ht_sb", [D + 1, TB * P], F32, own)
        turned = k.ps(tag + "_tp", [P, 1024], F32, own)
        made = k.ps(tag + "_mp", [P, 1024], F32, own)
        block = own.enter_context(nc.Block())

        @block.sync
        def _(sp):
            sp.dma_start(w_sb[:], w_d).then_inc(s_w, 16)

        @block.vector
        def _(dve):
            dve.memset(ht[D:D + 1, :], 1.0).then_inc(s_one, 1)
            with dve.Fori(0, NT // TB) as i:
                dve.tensor_copy(stage[:], h[:, bass.ds(i * TB, TB), :]).then_inc(s_stage, 1)
                dve.wait_ge(s_mm, i + 1)
                dve.tensor_copy(out[:, bass.ds(i * TB, TB), 0:width],
                                made[:, 0:TB * P].rearrange("p (t f) -> p t f", f=P)[:, :, 0:width]).then_inc(s_out, 1)

        @block.tensor
        def _(pe):
            pe.wait_ge(s_w, 16)
            pe.wait_ge(s_one, 1)
            with pe.Fori(0, NT // TB) as i:
                pe.wait_ge(s_stage, i + 1)
                pe.nop(nofuse=True)
                for j in range(TB):
                    last = pe.transpose(turned[0:D, j * P:(j + 1) * P], stage[:, j, :], ident[:])
                last.then_inc(s_tr, 1)
                pe.wait_ge(s_ht, i + 1)
                for j in range(TB):
                    last = pe.matmul(made[:, j * P:j * P + width], ht[:, j * P:(j + 1) * P], w_sb[:],
                                     start=True, stop=True)
                last.then_inc(s_mm, 1)

        @block.scalar
        def _(act):
            with act.Fori(0, NT // TB) as i:
                act.wait_ge(s_tr, i + 1)
                act.activation(ht[0:D, :], turned[0:D, 0:TB * P], ACT.Copy).then_inc(s_ht, 1)


@phase
def visit_list(nc, k, dstr_d, dst16_d, code_d, turns_sb, scr_d, ident):
    s_in, s_pad, s_16, s_mm, s_rt, s_bc = (k.sem("vl_" + x) for x in ("in", "pad", "i16", "minmax", "round", "bcast"))
    s_code, s_tr, s_c, s_out, s_io = (k.sem("vl_" + x) for x in ("code", "turned", "codei", "stored", "iota"))
    full = NG // P
    with ExitStack() as own:
        sb = lambda n, s, d=F32: k.sb("vl_" + n, s, d, own)
        dst = sb("dst", [P, NGC, GE], I32)
        dst16 = sb("dst16", [P, NGC, GE], I16)
        lohi = sb("lohi", [P, 2, NGC])
        lohi_i = sb("lohi_i", [P, 2, NGC], I32)
        table = sb("table", [P, 2, NGP])
        ends = sb("ends", [P, NGP])
        starts = sb("starts", [P, NGP])
        base = sb("base", [P, NGP])
        step = sb("step", [P, NGP])
        junk = sb("junk", [P, NGP])
        zero = sb("zero", [P, NGP])
        rank = sb("rank", [P, VCOLS])
        grp = sb("grp", [P, VCOLS])
        off = sb("off", [P, VCOLS])
        ok = sb("ok", [P, VCOLS])
        turns_f = sb("turns_f", [P, 2])
        cols_i = sb("cols_i", [P, 2], I32)
        code_i = sb("code_i", [P, 2, P], I32)
        lead_i = sb("lead_i", [1, LEAD], I32)
        tp = k.ps("vl_tp", [P, 2, P], F32, own)
        block = own.enter_context(nc.Block())

        @block.sync
        def _(sp):
            sp.wait_ge(s_pad, 1)
            rows = dstr_d.rearrange("(g e) -> g e", e=GE)
            sp.dma_start(dst[:, 0:full, :], rows[0:full * P, :].rearrange("(a p) e -> p a e", p=P)).then_inc(s_in, 16)
            sp.dma_start(dst[0:NG - full * P, full, :], rows[full * P:NG, :]).then_inc(s_in, 16)
            sp.wait_ge(s_16, 1)
            rows16 = dst16_d.rearrange("(g e) -> g e", e=GE)
            sp.dma_start(rows16[0:full * P, :].rearrange("(a p) e -> p a e", p=P), dst16[:, 0:full, :]).then_inc(s_out, 16)
            sp.dma_start(rows16[full * P:NG, :], dst16[0:NG - full * P, full, :]).then_inc(s_out, 16)
            sp.wait_ge(s_mm, 1)
            with nc.allow_non_contiguous_dma(reason="one word per group, once"):
                sp.dma_start(scr_d.rearrange("(r a p) -> p r a", p=P, r=2), lohi[:]).then_inc(s_rt, 16)
            sp.wait_ge(s_rt, 16)
            sp.dma_start(table[:], scr_d.rearrange("(o r g) -> o r g", o=1, r=2).to_broadcast([P, 2, NGP])).then_inc(s_bc, 16)
            sp.wait_ge(s_c, 1)
            lo = P * P
            sp.dma_start(code_d[LEAD:LEAD + lo].rearrange("(a b) -> a b", b=P), code_i[:, 0, :]).then_inc(s_out, 16)
            sp.dma_start(code_d[LEAD + lo:LEAD + VTAB].rearrange("(a b) -> a b", b=P), code_i[0:VCOLS - P, 1, :]).then_inc(s_out, 16)
            sp.dma_start(code_d[0:LEAD].rearrange("(a b) -> a b", a=1), lead_i[:]).then_inc(s_out, 16)
            sp.wait_ge(s_out, 80)

        @block.gpsimd
        def _(pool):
            pool.iota(rank[:], [[P, VCOLS]], base=0, channel_multiplier=1,
                      allow_small_or_imprecise_dtypes=True).then_inc(s_io, 1)

        @block.vector
        def _(dve):
            dve.memset(dst[:, full, :], 0)
            dve.drain().then_inc(s_pad, 1)
            dve.memset(lead_i[:], IDLE)
            dve.memset(zero[:], 0.0)
            dve.memset(grp[:], 0.0)
            dve.memset(off[:], 0.0)
            dve.wait_ge(s_in, 32)
            dve.tensor_copy(dst16[:], dst[:]).then_inc(s_16, 1)
            dve.tensor_reduce(lohi_i[:, 0, :], dst[:], AX.X, ALU.min)
            dve.tensor_reduce(lohi_i[:, 1, :], dst[:], AX.X, ALU.max)
            dve.drain()
            dve.tensor_scalar(lohi_i[:], lohi_i[:], 7, None, ALU.arith_shift_right)
            dve.drain()
            dve.tensor_copy(lohi[:], lohi_i[:])
            dve.drain()
            dve.scalar_tensor_tensor(lohi[:, 1, :], lohi[:, 1, :], 1.0, lohi[:, 0, :], ALU.add, ALU.subtract)
            dve.drain().then_inc(s_mm, 1)
            dve.wait_ge(s_bc, 16)
            dve.memset(table[:, 1, NG:NGP], 0.0)
            dve.memset(table[:, 0, NG:NGP], 0.0)
            dve.drain()
            dve.tensor_tensor_scan(ends[:], table[:, 1, :], zero[:], 0.0, ALU.add, ALU.add)
            dve.drain()
            dve.tensor_tensor(starts[:], ends[:], table[:, 1, :], ALU.subtract)
            dve.drain()
            dve.tensor_tensor(base[:], starts[:], table[:, 0, :], ALU.subtract)
            dve.drain()
            dve.tensor_tensor(step[:, 1:NGP], base[:, 1:NGP], base[:, 0:NGP - 1], ALU.subtract)
            dve.tensor_copy(step[:, 0:1], base[:, 0:1])
            dve.tensor_scalar(turns_f[:, 0:1], ends[:, NGP - 1:NGP], float(DRAIN + RING - 1), None, ALU.add)
            dve.tensor_scalar(turns_f[:, 1:2], ends[:, NGP - 1:NGP], float(DRAIN + RING - 1 + P), None, ALU.add)
            dve.drain()
            dve.tensor_copy(cols_i[:], turns_f[:])
            dve.drain()
            dve.tensor_scalar(turns_sb[:], cols_i[:, 0:1], RING.bit_length() - 1, None, ALU.arith_shift_right)
            dve.tensor_scalar(cols_i[:, 1:2], cols_i[:, 1:2], 7, None, ALU.arith_shift_right)
            dve.drain()
            dve.wait_ge(s_io, 1)
            cols = dve.value_load(cols_i[0:1, 1:2], min_val=1, max_val=VCOLS)
            with dve.Fori(0, cols) as j:
                dve.tensor_scalar(junk[:], ends[:], rank[:, bass.ds(j, 1)], 0.0, ALU.is_le, ALU.add,
                                  accum_out=grp[:, bass.ds(j, 1)])
                dve.drain()
                dve.scalar_tensor_tensor(junk[:], starts[:], rank[:, bass.ds(j, 1)], step[:], ALU.is_le, ALU.mult,
                                         accum_out=off[:, bass.ds(j, 1)])
                dve.drain()
            dve.tensor_scalar(ok[:], rank[:], ends[:, NGP - 1:NGP], None, ALU.is_lt)
            dve.tensor_tensor(off[:], rank[:], off[:], ALU.subtract)
            dve.drain()
            dve.tensor_scalar(off[:], off[:], float(-IDLE), None, ALU.add)
            dve.drain()
            dve.scalar_tensor_tensor(grp[:], grp[:], float(CODE), off[:], ALU.mult, ALU.add)
            dve.drain()
            dve.tensor_tensor(grp[:], grp[:], ok[:], ALU.mult)
            dve.drain()
            dve.tensor_scalar(grp[:], grp[:], float(IDLE), None, ALU.add)
            dve.drain().then_inc(s_code, 1)
            dve.wait_ge(s_tr, 1)
            dve.tensor_copy(code_i[:, 0, :], tp[:, 0, :])
            dve.tensor_copy(code_i[0:VCOLS - P, 1, :], tp[0:VCOLS - P, 1, :])
            dve.drain().then_inc(s_c, 1)

        @block.tensor
        def _(pe):
            pe.wait_ge(s_code, 1)
            pe.transpose(tp[:, 0, :], grp[:, 0:P], ident[:])
            pe.transpose(tp[0:VCOLS - P, 1, :], grp[:, P:VCOLS], ident[:]).then_inc(s_tr, 1)


def split3(dve, src, parts, rest):
    dve.tensor_copy(parts(0), src)
    dve.drain()
    dve.tensor_tensor(rest, src, parts(0), ALU.subtract)
    dve.drain()
    dve.tensor_copy(parts(1), rest)
    dve.drain()
    dve.tensor_tensor(rest, rest, parts(1), ALU.subtract)
    dve.drain()
    dve.tensor_copy(parts(2), rest)
    dve.drain()


@phase
def gat_tables(nc, k, tag, xlr, xr3, rows_d):
    s_row, s_out = k.sem(tag + "_rows"), k.sem(tag + "_rows_out")
    with ExitStack() as own:
        rows = k.sb(tag + "_rows_sb", [P, NT, ROW], F32, own)
        rest = k.sb(tag + "_rest", [P, NT, D], F32, own)
        block = own.enter_context(nc.Block())
        parts = rows[:, :, D + 2:ROW].bitcast(BF16)

        @block.vector
        def _(dve):
            dve.memset(xr3[:], 0.0)
            dve.memset(rows[:], 0.0)
            dve.drain()
            dve.memset(rows[:, :, D:D + 1], 1.0)
            dve.tensor_copy(rows[:, :, 0:D], xlr[:, :, 0:D])
            split3(dve, xlr[:, :, 0:D], lambda j: parts[:, :, j * D:(j + 1) * D], rest[:])
            dve.drain().then_inc(s_row, 1)
            split3(dve, xlr[:, :, D:2 * D], lambda j: xr3[:, 0:NT, j, :], rest[:])

        @block.sync
        def _(sp):
            sp.wait_ge(s_row, 1)
            sp.dma_start(rows_d.rearrange("(t p) f -> p t f", p=P), rows[:]).then_inc(s_out, 16)
            sp.wait_ge(s_out, 16)


@phase
def gat_edges(nc, k, tag, ea_d, src_d, dst16_d, code_d, rows_d, we_d, att_d, xr3, acc, ident, identb,
              iota_node, turns_sb):
    names = ("masked", "message", "relu", "score", "top", "weight", "turned", "evac", "sum", "acc")
    s = {n: k.sem(f"{tag}_{n}") for n in names}
    delay = {"masked": 0, "message": 1, "relu": 1, "score": 2, "top": 2, "weight": 2, "turned": 3,
             "evac": 3, "sum": 4, "acc": 5}
    s_ld = [k.sem(f"{tag}_in{j}") for j in range(RING)]
    s_g = [k.ctx.enter_context(nc.semaphore(f"{tag}_rows{j}")) for j in range(RING)]
    s_set, s_tab, s_w = k.sem(tag + "_set"), k.sem(tag + "_tab"), k.sem(tag + "_wts")

    def count(name, step, visit_delay):
        return step - visit_delay + delay[name] + 1 + FREE

    with ExitStack() as own:
        sb = lambda n, sh, d=F32: k.sb(f"{tag}_{n}", sh, d, own)
        codes = sb("codes", [1, LEAD + VTAB], I32)
        idx = sb("idx", [P, RING, GC], I32)
        rows = sb("rows", [P, RING, GC, ROW])
        dstb = sb("dstb", [P, RING, GE], I16)
        ea = sb("ea", [P, RING, GE // 2])
        hit = sb("hit", [P, 2, GE], BF16)
        miss = sb("miss", [P, 4, GE], BF16)
        xr = sb("xr", [P, 2, 3, D], BF16)
        relu = sb("relu", [P, 2, GE // 2])
        masked = sb("masked", [P, 2, GE])
        wts = sb("weights", [P, 2, GE])
        wtsT = sb("weightsT", [P, 2, GE])
        gmax = sb("gmax", [P, 2])
        newtop = sb("newtop", [P, 2])
        negtop = sb("negtop", [P, 2])
        fall = sb("fall", [P, 2])
        shrink = sb("shrink", [P, 4])
        top = sb("top", [P, NT + 1])
        we = sb("we", [P, P])
        att = sb("att", [P, 2, P])
        half = lambda t, j, c: t[64 * (c // 2):64 * (c // 2) + 64, j]
        mps = [k.ps(f"{tag}_mps{j}", [P, 512], F32, own) for j in range(2)]
        sps = [k.ps(f"{tag}_sps{j}", [P, 512], F32, own) for j in range(2)]
        tps = [k.ps(f"{tag}_tps{j}", [P, 512], F32, own) for j in range(2)]
        aps = [k.ps(f"{tag}_aps{j}", [P, 512], F32, own) for j in range(2)]
        block = own.enter_context(nc.Block())

        @block.sync
        def _(sp):
            sp.dma_start(codes[:], code_d.rearrange("(a b) -> a b", a=1)).then_inc(s_tab, 16)
            sp.dma_start(we[:], we_d).then_inc(s_w, 16)
            sp.dma_start(att[:], att_d).then_inc(s_w, 16)
            sp.wait_ge(s_tab, 16)
            sp.wait_ge(s_set, 3)
            group = sp.alloc_register(tag + "_group")
            turns = sp.value_load(turns_sb[0:1, 0:1], min_val=1, max_val=VTAB // RING)
            with sp.Fori(0, turns) as i:
                for u in range(RING):
                    step = i * RING + u
                    code = sp.value_load(codes[0:1, bass.ds(step + LEAD, 1)], min_val=0, max_val=NG * CODE - 1)
                    sp.reg_alu(group, code, CODE.bit_length() - 1, ALU.logical_shift_right)
                    g = sp.snap(group, min_val=0, max_val=NG - 1)
                    sp.wait_ge(s["sum"], count("sum", step, RING))
                    sp.dma_start(idx[:, u, :], src_d[bass.ds(g, 1), :, :]).then_inc(s_ld[u], 16)
                    sp.dma_start(dstb[:, u, :], dst16_d[bass.ds(g, 1), :].to_broadcast([P, GE])).then_inc(s_ld[u], 16)
                    sp.dma_start(ea[:, u, :], ea_d[bass.ds(g, 1), :, :]).then_inc(s_ld[u], 16)

        @block.gpsimd
        def _(pool):
            turns = pool.value_load(turns_sb[0:1, 0:1], min_val=1, max_val=VTAB // RING)
            pool.wait_ge(s_set, 3)
            with pool.Fori(0, turns) as i:
                for u in range(RING):
                    pool.wait_ge(s_ld[u], i * 48 + 48)
                    pool.nop(nofuse=True)
                    for c in range(GC):
                        pool.indirect_dma_start(rows[:, u, c, :], None, rows_d,
                                                bass.IndirectOffsetOnAxis(ap=idx[:, u, c:c + 1], axis=0)
                                                ).then_inc(s_g[u], 16)

        @block.vector
        def _(dve):
            dve.memset(rows[:], 0.0)
            dve.memset(hit[:], 0.0)
            dve.memset(xr[:], 0.0)
            dve.memset(miss[:], 0.0)
            dve.memset(relu[:], 0.0)
            dve.memset(ea[:], 0.0)
            dve.memset(masked[:], MASK)
            dve.memset(wts[:], 0.0)
            dve.memset(wtsT[:], 0.0)
            dve.memset(negtop[:], 0.0)
            dve.memset(fall[:], 0.0)
            dve.memset(shrink[:], 0.0)
            dve.memset(acc[:], 0.0)
            dve.memset(top[:], FLOOR)
            for bank in aps:
                dve.memset(bank[:, 0:D + 1], 0.0)
            dve.drain().then_inc(s_set, 1)
            for n in ("masked", "relu", "top", "acc"):
                dve.sem_inc(s[n], FREE)
            dve.wait_ge(s_set, 3)
            dve.wait_ge(s_tab, 16)
            turns = dve.value_load(turns_sb[0:1, 0:1], min_val=1, max_val=VTAB // RING)
            carry = [dve.alloc_register(f"{tag}_t{j}") for j in range(DRAIN)]
            fresh = [dve.alloc_register(f"{tag}_f{j}") for j in range(RING)]
            for r in carry:
                dve.reg_mov(r, IDLE)
            with dve.Fori(0, turns) as i:
                tiles = [dve.snap(r, min_val=0, max_val=IDLE) for r in carry]
                for u in range(RING):
                    step = i * RING + u
                    code = dve.value_load(codes[0:1, bass.ds(step + LEAD, 1)], min_val=0, max_val=NG * CODE - 1)
                    dve.reg_alu(fresh[u], code, CODE - 1, ALU.bitwise_and)
                    tiles.append(dve.snap(fresh[u], min_val=0, max_val=IDLE))
                    t = tiles[-1]
                    tm, ta = tiles[-3], tiles[-6]
                    node = iota_node[:, bass.ds(t, 1)]
                    dve.wait_ge(s_ld[u], i * 48 + 48)
                    dve.wait_ge(s_g[u], i * (16 * GC) + 16 * GC)
                    dve.wait_ge(s["message"], count("message", step, 2))
                    dve.tensor_copy(xr[:, u % 2, :, :], xr3[:, bass.ds(t, 1), :, :].rearrange("p a q f -> p (a q) f"))
                    dve.tensor_scalar(hit[:, u % 2, :], dstb[:, u, :], node, None, ALU.is_equal)
                    dve.tensor_scalar(miss[:, u % 4, :], dstb[:, u, :], node, MASK, ALU.not_equal, ALU.mult
                                      ).then_inc(s["masked"], 1)
                    dve.wait_ge(s["message"], count("message", step, 1))
                    dve.tensor_copy(relu[:, (u - 1) % 2, :], mps[(u - 1) % 2][:, 0:GE // 2])
                    dve.wait_ge(s["score"], count("score", step, 2))
                    dve.wait_ge(s["weight"], count("weight", step, 4))
                    dve.nop(nofuse=True)
                    j = (u - 2) % 2
                    dve.drain()
                    dve.scalar_tensor_tensor(relu[:, (u - 1) % 2, :], relu[:, (u - 1) % 2, :], 0.2,
                                             relu[:, (u - 1) % 2, :], ALU.mult, ALU.max).then_inc(s["relu"], 1)
                    dve.tensor_tensor_reduce(masked[:, j, :], sps[j][:], miss[:, (u - 2) % 4, :], 1.0, FLOOR,
                                             ALU.add, ALU.max, accum_out=gmax[:, j:j + 1])
                    dve.wait_ge(s["sum"], count("sum", step, 5))
                    a = acc[:, bass.ds(ta, 1), :].rearrange("p a f -> p (a f)")
                    dve.scalar_tensor_tensor(a, a, shrink[:, (u - 5) % 4:(u - 5) % 4 + 1],
                                             aps[(u - 5) % 2][:, 0:D + 1], ALU.mult, ALU.add).then_inc(s["acc"], 1)
                    dve.drain()
                    dve.tensor_tensor(newtop[:, j:j + 1], top[:, bass.ds(tm, 1)], gmax[:, j:j + 1], ALU.max)
                    dve.drain()
                    dve.tensor_scalar(negtop[:, j:j + 1], newtop[:, j:j + 1], -1.0, None, ALU.mult)
                    dve.tensor_tensor(fall[:, j:j + 1], top[:, bass.ds(tm, 1)], newtop[:, j:j + 1], ALU.subtract)
                    dve.drain().then_inc(s["top"], 1)
                    dve.tensor_copy(top[:, bass.ds(tm, 1)], newtop[:, j:j + 1])
                for r, t in zip(carry, tiles[-DRAIN:]):
                    dve.reg_mov(r, t)

        @block.scalar
        def _(act):
            for n in ("weight", "evac"):
                act.sem_inc(s[n], FREE)
            act.sem_inc(s_set, 1)
            act.wait_ge(s_set, 3)
            turns = act.value_load(turns_sb[0:1, 0:1], min_val=1, max_val=VTAB // RING)
            with act.Fori(0, turns) as i:
                for u in range(RING):
                    step = i * RING + u
                    j = (u - 2) % 2
                    act.wait_ge(s["top"], count("top", step, 2))
                    act.wait_ge(s["turned"], count("turned", step, 4))
                    act.activation(wts[:, j, :], masked[:, j, :], ACT.Exp, bias=negtop[:, j:j + 1])
                    act.wait_ge(s["acc"], count("acc", step, 6))
                    act.activation(shrink[:, (u - 2) % 4:(u - 2) % 4 + 1], fall[:, j:j + 1], ACT.Exp)
                    act.drain().then_inc(s["weight"], 1)
                    j = (u - 3) % 2
                    act.wait_ge(s["turned"], count("turned", step, 3))
                    act.wait_ge(s["sum"], count("sum", step, 5))
                    act.activation(wtsT[:, j, :], tps[j][:], ACT.Copy).then_inc(s["evac"], 1)

        @block.tensor
        def _(pe):
            pe.wait_ge(s_w, 32)
            for n in ("message", "score", "turned", "sum"):
                pe.sem_inc(s[n], FREE)
            pe.sem_inc(s_set, 1)
            pe.wait_ge(s_set, 3)
            turns = pe.value_load(turns_sb[0:1, 0:1], min_val=1, max_val=VTAB // RING)
            with pe.Fori(0, turns) as i:
                for u in range(RING):
                    step = i * RING + u
                    v, j = (u - 1) % RING, (u - 1) % 2
                    pe.wait_ge(s["masked"], count("masked", step, 1))
                    pe.wait_ge(s["relu"], count("relu", step, 3))
                    pe.matmul(mps[j][:, 0:GE // 2], we[:], ea[:, v, :], start=True, stop=False)
                    for h in range(2):
                        for q in range(3):
                            pe.matmul(mps[j][64 * h:64 * h + 64, 0:GE // 2],
                                      xr[:, j, q, :],
                                      hit[:, j, h * (GE // 2):(h + 1) * (GE // 2)], start=False, stop=False)
                    for c in range(GC):
                        part = rows[:, v, c, D + 2:ROW].bitcast(BF16)
                        for q in range(3):
                            last = pe.matmul(mps[j][64 * (c // 2):64 * (c // 2) + 64, P * (c % 2):P * (c % 2) + P],
                                             part[:, q * D:(q + 1) * D], identb[:], start=False,
                                             stop=(c % 2 == 1 and q == 2))
                    last.then_inc(s["message"], 1)
                    j = (u - 2) % 2
                    pe.wait_ge(s["relu"], count("relu", step, 2))
                    pe.wait_ge(s["top"], count("top", step, 4))
                    for h in range(2):
                        last = pe.matmul(sps[j][:, h * (GE // 2):(h + 1) * (GE // 2)], att[:, h, :], relu[:, j, :],
                                         start=True, stop=True)
                    last.then_inc(s["score"], 1)
                    j = (u - 3) % 2
                    pe.wait_ge(s["weight"], count("weight", step, 3))
                    pe.wait_ge(s["evac"], count("evac", step, 5))
                    for c in range(GC):
                        last = pe.transpose(tps[j][:, c * P:(c + 1) * P], wts[:, j, c * P:(c + 1) * P], ident[:])
                    last.then_inc(s["turned"], 1)
                    j, v = (u - 4) % 2, (u - 4) % RING
                    pe.wait_ge(s["evac"], count("evac", step, 4))
                    pe.wait_ge(s["acc"], count("acc", step, 6))
                    for c in range(GC):
                        last = pe.matmul(aps[j][:, 0:D + 1], wtsT[:, j, c * P:(c + 1) * P], rows[:, v, c, 0:D + 1],
                                         start=(c == 0), stop=(c == GC - 1))
                    last.then_inc(s["sum"], 1)


def gat_mean(nc, k, acc, out, bias_sb, st, add=None):
    with nc.Block() as block:
        @block.vector
        def _(dve):
            dve.tensor_scalar(st[:, 0, :], acc[:, :, D], 1e-16, None, ALU.add)
            dve.drain()
            dve.reciprocal(st[:, 1, :], st[:, 0, :])
            dve.drain()
            dve.tensor_tensor(out[:], acc[:, 0:NT, 0:D], per_node(st[:, 1, :]), ALU.mult)
            dve.drain()
            dve.tensor_tensor(out[:], out[:], bias_sb[:].unsqueeze(1).to_broadcast([P, NT, D]), ALU.add)
            if add is not None:
                dve.drain()
                dve.tensor_tensor(out[:], out[:], add[:], ALU.add)


@phase
def adjacency(nc, k, dstr_d, srcc_d, dstc_d, adj_d, mm_d, wt_d):
    s_in, s_mm, s_rt, s_bc, s_win, s_wt, s_tab = (k.sem("adj_" + x) for x in
                                                  ("in", "mm", "round", "bcast", "win", "wt", "tab"))
    s_cols, s_iota, s_set = k.sem("adj_cols"), k.sem("adj_iota"), k.sem("adj_set")
    s_hot, s_used, s_win_done, s_evac, s_st, s_at = (k.sem("adj_" + x) for x in
                                                     ("hot", "used", "window", "evac", "stored", "tile_free"))
    BIG = 4096.0
    with ExitStack() as own:
        sb = lambda n, s, d=F32: k.sb("adj_" + n, s, d, own)
        low = sb("low", [P, NQ * CT])
        key = sb("key", [P, NQ * CT])
        winbase = sb("winbase", [P, NW + 1])
        iota_lo = sb("iota_lo", [P, P], I16)
        iota_key = sb("iota_key", [P, WD * NT], I16)
        hot_lo = sb("hot_lo", [P, CT, P], BF16)
        hot_key = sb("hot_key", [P, CT, WD * NT], BF16)
        zero = sb("zero", [P, WB * NT], BF16)
        base = sb("base", [P, 2])
        wtab = sb("wtab", [1, NWP], I32)
        tiles = sb("tiles", [P, 2, NT, P // WD, WD], BF16)
        banks = [[k.ps(f"adj_b{j}{m}", [P, 512], F32, own) for m in range(WD // WB)] for j in range(2)]
        with ExitStack() as prep:
            pb = lambda n, s, d=F32: k.sb("adjp_" + n, s, d, prep)
            dst = pb("dst", [P, NCC, P], I32)
            src_i = pb("src", [P, NQ * CT], I32)
            dst_i = pb("dstc", [P, NQ * CT], I32)
            part = pb("part", [P, NQ * CT], I32)
            mm = pb("mm", [P, 2, NCC])
            ranges = pb("ranges", [P, 2, NCC * P])
            cond = pb("cond", [P, NQ * CT])
            junk = pb("junk", [P, NQ * CT])
            up = pb("up", [P, NQ * CT])
            down = pb("down", [P, NQ * CT])
            wlo = pb("wlo", [P, NWC])
            whi = pb("whi", [P, NWC])
            first = pb("first", [P, NWC])
            last = pb("last", [P, NWC])
            win_i = pb("win_i", [P, 2, NWC], I32)
            full = NQ * CT // P
            block = prep.enter_context(nc.Block())

            @block.sync
            def _(sp):
                sp.wait_ge(s_set, 1)
                rows = dstr_d.rearrange("(c e) -> c e", e=P)
                sp.dma_start(dst[:, 0:full, :], rows[0:full * P, :].rearrange("(a p) e -> p a e", p=P)).then_inc(s_in, 16)
                sp.dma_start(dst[0:NQ * CT - full * P, full, :], rows[full * P:NQ * CT, :]).then_inc(s_in, 16)
                sp.dma_start(src_i[:], srcc_d).then_inc(s_cols, 16)
                sp.dma_start(dst_i[:], dstc_d).then_inc(s_cols, 16)
                sp.wait_ge(s_mm, 1)
                with nc.allow_non_contiguous_dma(reason="one word per chunk, once"):
                    sp.dma_start(mm_d.rearrange("(r a p) -> p r a", p=P, r=2), mm[:]).then_inc(s_rt, 16)
                sp.wait_ge(s_rt, 16)
                sp.dma_start(ranges[:], mm_d.rearrange("(o r g) -> o r g", o=1, r=2).to_broadcast([P, 2, NCC * P])).then_inc(s_bc, 16)
                sp.wait_ge(s_win, 1)
                with nc.allow_non_contiguous_dma(reason="one word per window, once"):
                    sp.dma_start(wt_d.rearrange("(a p) -> p a", p=P), win_i[:, 0, :]).then_inc(s_wt, 16)
                sp.wait_ge(s_wt, 16)
                sp.dma_start(wtab[:], wt_d.rearrange("(o w) -> o w", o=1)).then_inc(s_tab, 16)
                sp.wait_ge(s_tab, 16)

            @block.gpsimd
            def _(pool):
                f = dict(allow_small_or_imprecise_dtypes=True)
                pool.iota(iota_lo[:], [[1, P]], base=0, channel_multiplier=0, **f)
                pool.iota(iota_key[:], [[1, WD * NT]], base=0, channel_multiplier=0, **f)
                pool.iota(up[:], [[1, NQ * CT]], base=1, channel_multiplier=0, **f)
                pool.iota(wlo[:], [[WD * P, NWC]], base=0, channel_multiplier=WD, **f)
                pool.iota(winbase[:], [[WD * NT, NW + 1]], base=0, channel_multiplier=0, **f)
                pool.drain().then_inc(s_iota, 1)

            @block.vector
            def _(dve):
                dve.memset(dst[:, full, :], 0)
                dve.drain().then_inc(s_set, 1)
                dve.memset(zero[:], 0.0)
                dve.wait_ge(s_in, 32)
                dve.tensor_reduce(mm[:, 0, :], dst[:], AX.X, ALU.min)
                dve.tensor_reduce(mm[:, 1, :], dst[:], AX.X, ALU.max)
                dve.drain().then_inc(s_mm, 1)
                dve.wait_ge(s_cols, 32)
                dve.tensor_scalar(part[:], src_i[:], P - 1, None, ALU.bitwise_and)
                dve.drain()
                dve.tensor_copy(low[:], part[:])
                dve.drain()
                dve.tensor_scalar(part[:], src_i[:], 7, None, ALU.arith_shift_right)
                dve.tensor_copy(key[:], dst_i[:])
                dve.drain()
                dve.scalar_tensor_tensor(key[:], key[:], float(NT), part[:], ALU.mult, ALU.add)
                dve.wait_ge(s_iota, 1)
                dve.tensor_scalar(down[:], up[:], -1.0, BIG + 1.0, ALU.mult, ALU.add)
                dve.tensor_scalar(whi[:], wlo[:], float(WD - 1), None, ALU.add)
                dve.drain()
                dve.wait_ge(s_bc, 16)
                for a in range(NWC):
                    dve.tensor_scalar(junk[:], ranges[:, 1, 0:NQ * CT], wlo[:, a:a + 1], None, ALU.is_ge)
                    dve.drain()
                    dve.scalar_tensor_tensor(cond[:], ranges[:, 0, 0:NQ * CT], whi[:, a:a + 1], junk[:], ALU.is_le, ALU.mult)
                    dve.drain()
                    dve.tensor_tensor_reduce(junk[:], cond[:], down[:], 1.0, 0.0, ALU.mult, ALU.max, accum_out=first[:, a:a + 1])
                    dve.drain()
                    dve.tensor_tensor_reduce(junk[:], cond[:], up[:], 1.0, 0.0, ALU.mult, ALU.max, accum_out=last[:, a:a + 1])
                    dve.drain()
                dve.tensor_scalar(first[:], first[:], -1.0, BIG, ALU.mult, ALU.add)
                dve.tensor_scalar(last[:], last[:], 1.0, None, ALU.max)
                dve.drain()
                dve.tensor_scalar(junk[:, 0:NWC], last[:], -1.0, None, ALU.add)
                dve.drain()
                dve.tensor_tensor(first[:], first[:], junk[:, 0:NWC], ALU.min)
                dve.tensor_scalar(last[:], last[:], float(CT - 1), None, ALU.add)
                dve.drain()
                dve.tensor_copy(win_i[:, 0, :], first[:])
                dve.tensor_copy(win_i[:, 1, :], last[:])
                dve.drain()
                dve.tensor_scalar(win_i[:], win_i[:], CT.bit_length() - 1, None, ALU.arith_shift_right)
                dve.drain()
                dve.tensor_scalar(first[:], win_i[:, 0, :], float(PACK), None, ALU.mult)
                dve.drain()
                dve.tensor_tensor(win_i[:, 0, :], first[:], win_i[:, 1, :], ALU.add)
                dve.drain().then_inc(s_win, 1)

        def chunk_turns(eng, regs, w):
            code = eng.value_load(wtab[0:1, bass.ds(w, 1)], min_val=1, max_val=NQ * PACK)
            eng.reg_alu(regs[0], code, PACK.bit_length() - 1, ALU.logical_shift_right)
            eng.reg_alu(regs[1], code, PACK - 1, ALU.bitwise_and)
            return eng.snap(regs[0], min_val=0, max_val=NQ - 1), eng.snap(regs[1], min_val=1, max_val=NQ)

        block = own.enter_context(nc.Block())

        @block.vector
        def _(dve):
            turn = dve.alloc_register("adj_dve_turns")
            ends = [dve.alloc_register(f"adj_dve_end{b}") for b in range(2)]
            dve.reg_mov(turn, 1)
            dve.tensor_copy(base[:, 0:1], winbase[:, 0:1])
            with dve.Fori(0, NW // 2) as i:
                for m in range(2):
                    w = i * 2 + m
                    q0, q1 = chunk_turns(dve, ends, w)
                    dve.drain()
                    dve.tensor_copy(base[:, 1 - m:2 - m], winbase[:, bass.ds(w + 1, 1)])
                    with dve.Fori(q0, q1) as q:
                        done = dve.snap(turn, min_val=1, max_val=1 << 24)
                        for b in range(CT):
                            c = dve.snap(q * CT + b, min_val=0, max_val=NQ * CT - 1)
                            dve.wait_ge(s_used, done * CT + b)
                            dve.tensor_scalar(hot_lo[:, b, :], iota_lo[:], low[:, bass.ds(c, 1)], None, ALU.is_equal)
                            dve.tensor_scalar(hot_key[:, b, :], iota_key[:], base[:, m:m + 1], key[:, bass.ds(c, 1)],
                                              ALU.add, ALU.is_equal).then_inc(s_hot, 1)
                        dve.reg_add(turn, turn, 1)

        @block.tensor
        def _(pe):
            pe.sem_inc(s_used, 2 * CT - 1)
            turn = pe.alloc_register("adj_pe_turns")
            ends = [pe.alloc_register(f"adj_pe_end{b}") for b in range(2)]
            pe.reg_mov(turn, 1)
            with pe.Fori(0, NW // 2) as i:
                for b in range(2):
                    w = i * 2 + b
                    q0, q1 = chunk_turns(pe, ends, w)
                    pe.wait_ge(s_evac, w + 1)
                    for bank in banks[b]:
                        pe.matmul(bank[:, 0:WB * NT], zero[:, 0:P], zero[:], start=True, stop=False)
                    with pe.Fori(q0, q1):
                        n = pe.snap(turn, min_val=1, max_val=1 << 24)
                        for c in range(CT):
                            pe.wait_ge(s_hot, n * CT + (c + 1 - CT))
                            for m, bank in enumerate(banks[b]):
                                last = pe.matmul(bank[:, 0:WB * NT], hot_lo[:, c, :],
                                                 hot_key[:, c, m * WB * NT:(m + 1) * WB * NT], start=False, stop=False)
                            last.then_inc(s_used, 1)
                        pe.reg_add(turn, turn, 1)
                    for bank in banks[b]:
                        last = pe.matmul(bank[:, 0:WB * NT], zero[:, 0:P], zero[:], start=False, stop=True)
                    last.then_inc(s_win_done, 1)

        @block.scalar
        def _(act):
            act.sem_inc(s_evac, 2)
            with act.Fori(0, NT) as t:
                act.wait_ge(s_at, t + 1)
                slot = act.snap(t & 1, min_val=0, max_val=1)
                with act.Fori(0, P // WD // 2) as i:
                    for b in range(2):
                        w = i * 2 + b
                        act.wait_ge(s_win_done, t * (P // WD) + w + 1)
                        for m, bank in enumerate(banks[b]):
                            to = tiles[:, bass.ds(slot, 1), :, bass.ds(w, 1), m * WB:(m + 1) * WB]
                            last = act.activation(to.rearrange("p a h w d -> p (a h) (w d)"),
                                                  bank[:, 0:WB * NT].rearrange("p (d h) -> p h d", h=NT), ACT.Copy)
                        last.then_inc(s_evac, 1)

        @block.sync
        def _(sp):
            sp.sem_inc(s_at, 2)
            with sp.Fori(0, NT) as t:
                sp.wait_ge(s_evac, t * (P // WD) + (P // WD + 2))
                slot = sp.snap(t & 1, min_val=0, max_val=1)
                sp.dma_start(adj_d[bass.ds(t, 1), :, :].rearrange("a p f -> (a p) f"),
                             tiles[:, bass.ds(slot, 1), :, :, :].rearrange("p a h w d -> p (a h w d)")).then_inc(s_st, 16)
                sp.wait_ge(s_st, t * 16 + 16)
                sp.sem_inc(s_at, 1)


@phase
def propagate(nc, k, tag, adj_d, parts, out, deg):
    PIECE = 7
    NPC = NT // PIECE
    s_in = [k.sem(f"{tag}_in{j}") for j in range(NPC)]
    s_mm, s_st, s_out, s_use = (k.sem(tag + x) for x in ("_mm", "_staged", "_out", "_used"))
    W = 3 * D + 1
    with ExitStack() as own:
        adj = k.sb(tag + "_adj", [P, NPC, PIECE * P], BF16, own)
        stage = k.sb(tag + "_stage", [P, 2, W], F32, own)
        tmp = k.sb(tag + "_tmp", [P, 2, D], F32, own)
        banks = [k.ps(f"{tag}_b{j}", [P, 512], F32, own) for j in range(2)]
        block = own.enter_context(nc.Block())

        @block.sync
        def _(sp):
            with sp.Fori(0, NT) as t:
                for c in range(NPC):
                    sp.wait_ge(s_use, t * NPC + (c + 1))
                    sp.dma_start(adj[:, c, :], adj_d[bass.ds(t, 1), :, c * PIECE * P:(c + 1) * PIECE * P]).then_inc(s_in[c], 16)

        @block.tensor
        def _(pe):
            pe.sem_inc(s_use, NPC)

            def tile(t, b):
                pe.wait_ge(s_st, t + 1)
                for c in range(NPC):
                    pe.wait_ge(s_in[c], t * 16 + 16)
                    for j in range(PIECE):
                        hi = c * PIECE + j
                        last = pe.matmul(banks[b][:, 0:W], adj[:, c, j * P:(j + 1) * P], parts[:, hi, :],
                                         start=(hi == 0), stop=(hi == NT - 1))
                    last.then_inc(s_use, 1)

            with pe.Fori(0, NT // 2) as i:
                for b in range(2):
                    tile(i * 2 + b, b)
            tile(NT - 1, 0)

        @block.scalar
        def _(act):
            act.sem_inc(s_st, 2)

            def tile(t, b):
                act.wait_ge(s_use, t * NPC + 2 * NPC)
                act.wait_ge(s_out, t + 1)
                act.activation(stage[:, b, :], banks[b][:, 0:W], ACT.Copy).then_inc(s_st, 1)

            with act.Fori(0, NT // 2) as i:
                for b in range(2):
                    tile(i * 2 + b, b)
            tile(NT - 1, 0)

        @block.vector
        def _(dve):
            dve.sem_inc(s_out, 2)

            def tile(t, b):
                dve.wait_ge(s_st, t + 3)
                dve.tensor_tensor(tmp[:, b, :], stage[:, b, D:2 * D], stage[:, b, 2 * D:3 * D], ALU.add)
                if deg is not None:
                    dve.tensor_copy(deg[:, bass.ds(t, 1)], stage[:, b, 3 * D:W])
                dve.drain()
                dve.tensor_tensor(out[:, bass.ds(t, 1), :].rearrange("p a f -> p (a f)"), stage[:, b, 0:D],
                                  tmp[:, b, :], ALU.add).then_inc(s_out, 1)

            with dve.Fori(0, NT // 2) as i:
                for b in range(2):
                    tile(i * 2 + b, b)
            tile(NT - 1, 0)


def to_parts(nc, k, tag, src, parts, scale=None):
    with ExitStack() as own:
        rest = k.sb(tag + "_rest", [P, NT, D], F32, own)
        block = own.enter_context(nc.Block())

        @block.vector
        def _(dve):
            if scale is not None:
                dve.tensor_tensor(src[:], src[:], per_node(scale), ALU.mult)
                dve.drain()
            dve.memset(parts[:, :, 3 * D:3 * D + 1], 1.0)
            split3(dve, src[:], lambda j: parts[:, :, j * D:(j + 1) * D], rest[:])


@phase
def mlp(nc, k, tag, h, wa_d, hid, wb_d, bias_row, out, ident):
    s_w, s_one, s_stage, s_tr, s_ht, s_m1, s_h2, s_mm = (k.sem(tag + x) for x in (
        "_w", "_one", "_staged", "_turned", "_ht", "_first", "_hidden", "_mm"))
    kb = hid + bias_row
    nodes = TB * P
    cut = [(0, 512), (512, nodes)]
    with ExitStack() as own:
        wa = k.sb(tag + "_wa", [D + 1, hid], F32, own)
        wb = k.sb(tag + "_wb", [kb, D], F32, own)
        stage = k.sb(tag + "_stage", [P, TB, D], F32, own)
        ht = k.sb(tag + "_ht_sb", [D + 1, nodes], F32, own)
        h2 = k.sb(tag + "_h2_sb", [kb, nodes], F32, own)
        turned = k.ps(tag + "_tp", [P, 1024], F32, own)
        hidden = k.ps(tag + "_hp", [P, 1024], F32, own)
        made = k.ps(tag + "_mp", [P, 512], F32, own)
        block = own.enter_context(nc.Block())

        @block.sync
        def _(sp):
            sp.dma_start(wa[:], wa_d).then_inc(s_w, 16)
            sp.dma_start(wb[:], wb_d).then_inc(s_w, 16)

        @block.vector
        def _(dve):
            dve.memset(ht[D:D + 1, :], 1.0)
            if bias_row:
                dve.memset(h2[hid:hid + 1, :], 1.0)
            dve.drain().then_inc(s_one, 1)
            with dve.Fori(0, NT // TB) as i:
                dve.tensor_copy(stage[:], h[:, bass.ds(i * TB, TB), :]).then_inc(s_stage, 1)
                dve.wait_ge(s_mm, i + 1)
                dve.nop(nofuse=True)
                dve.tensor_copy(out[:, bass.ds(i * TB, TB), 0:D],
                                made[:, 0:TB * D].rearrange("p (t f) -> p t f", f=D))
                dve.drain()

        @block.tensor
        def _(pe):
            pe.wait_ge(s_w, 32)
            pe.wait_ge(s_one, 1)
            with pe.Fori(0, NT // TB) as i:
                pe.wait_ge(s_stage, i + 1)
                pe.nop(nofuse=True)
                for j in range(TB):
                    last = pe.transpose(turned[0:D, j * P:(j + 1) * P], stage[:, j, :], ident[:])
                last.then_inc(s_tr, 1)
                pe.wait_ge(s_ht, i + 1)
                for a, b in cut:
                    last = pe.matmul(hidden[0:hid, a:b], wa[:], ht[:, a:b], start=True, stop=True)
                last.then_inc(s_m1, 1)
                pe.wait_ge(s_h2, i + 1)
                for j in range(TB):
                    last = pe.matmul(made[:, j * D:(j + 1) * D], h2[:, j * P:(j + 1) * P], wb[:], start=True, stop=True)
                last.then_inc(s_mm, 1)

        @block.scalar
        def _(act):
            with act.Fori(0, NT // TB) as i:
                act.wait_ge(s_tr, i + 1)
                act.activation(ht[0:D, :], turned[0:D, 0:nodes], ACT.Copy).then_inc(s_ht, 1)
                act.wait_ge(s_m1, i + 1)
                act.activation(h2[0:hid, :], hidden[0:hid, 0:nodes], ACT.Relu).then_inc(s_h2, 1)


@phase
def batch_norm(nc, k, z, h, x, ones, gb_d):
    s_g, s_sq, s_mm, s_var, s_sd, s_row, s_bp = (k.sem("bn_" + n) for n in
                                                 ("gb", "sq", "sums", "var", "sd", "row", "bcast"))
    lastp = N - (NT - 1) * P
    with ExitStack() as own:
        sb = lambda n, s: k.sb("bn_" + n, s, F32, own)
        sq = sb("sq", [P, NT, D])
        sums = sb("sums", [P, 2, D])
        gb = sb("gb", [1, 2, D])
        st = sb("st", [1, 6, D])
        row = sb("row", [1, 2, D])
        bc = sb("bc", [P, 2, D])
        tot = k.ps("bn_tot", [P, 512], F32, own)
        bp = k.ps("bn_bp", [P, 512], F32, own)
        block = own.enter_context(nc.Block())
        wide = lambda v: v.unsqueeze(1).to_broadcast([P, NT, D])

        @block.sync
        def _(sp):
            sp.dma_start(gb[:], gb_d.rearrange("(o a) b -> o a b", o=1)).then_inc(s_g, 16)

        @block.vector
        def _(dve):
            dve.memset(sums[:], 0.0)
            dve.tensor_tensor(sq[:], z[:], z[:], ALU.mult)
            dve.drain()
            dve.tensor_reduce(sums[:, 0, :], z[:, 0:NT - 1, :].rearrange("p t f -> p f t"), AX.X, ALU.add)
            dve.drain()
            dve.tensor_tensor(sums[0:lastp, 0, :], sums[0:lastp, 0, :], z[0:lastp, NT - 1, :], ALU.add)
            dve.drain().then_inc(s_sq, 1)
            dve.wait_ge(s_mm, 1)
            dve.tensor_scalar(bc[:, 0, :], tot[:, 0:D], 1.0 / N, None, ALU.mult)
            dve.drain()
            dve.tensor_tensor(z[:], z[:], wide(bc[:, 0, :]), ALU.subtract)
            dve.drain()
            dve.tensor_tensor(sq[:], z[:], z[:], ALU.mult)
            dve.drain()
            dve.tensor_reduce(sums[:, 1, :], sq[:, 0:NT - 1, :].rearrange("p t f -> p f t"), AX.X, ALU.add)
            dve.drain()
            dve.tensor_tensor(sums[0:lastp, 1, :], sums[0:lastp, 1, :], sq[0:lastp, NT - 1, :], ALU.add)
            dve.drain().then_inc(s_sq, 1)
            dve.wait_ge(s_mm, 2)
            dve.tensor_scalar(st[:, 0, :], tot[0:1, 64:64 + D], 1.0 / N, EPS, ALU.mult, ALU.add).then_inc(s_var, 1)
            dve.wait_ge(s_sd, 1)
            dve.reciprocal(st[:, 2, :], st[:, 1, :])
            dve.wait_ge(s_g, 16)
            dve.drain()
            dve.tensor_tensor(row[:, 0, :], st[:, 2, :], gb[:, 0, :], ALU.mult)
            dve.tensor_copy(row[:, 1, :], gb[:, 1, :])
            dve.drain().then_inc(s_row, 1)
            dve.wait_ge(s_bp, 1)
            dve.tensor_copy(bc[:], bp[:, 0:2 * D].rearrange("p (a f) -> p a f", a=2))
            dve.drain()
            dve.tensor_tensor(z[:], z[:], wide(bc[:, 0, :]), ALU.mult)
            dve.drain()
            dve.tensor_tensor(z[:], z[:], wide(bc[:, 1, :]), ALU.add)
            dve.drain()
            dve.scalar_tensor_tensor(z[:], z[:], 0.0, h[:], ALU.max, ALU.add)
            dve.drain()
            dve.tensor_tensor(x[:], x[:], z[:], ALU.add)

        @block.tensor
        def _(pe):
            for j in range(2):
                pe.wait_ge(s_sq, j + 1)
                pe.matmul(tot[:, 64 * j:64 * j + D], ones[:], sums[:, j, :], start=True, stop=True).then_inc(s_mm, 1)
            pe.wait_ge(s_row, 1)
            pe.matmul(bp[:, 0:2 * D], ones[0:1, :], row[:].rearrange("o a f -> o (a f)"), start=True, stop=True).then_inc(s_bp, 1)

        @block.scalar
        def _(act):
            act.wait_ge(s_var, 1)
            act.activation(st[:, 1, :], st[:, 0, :], ACT.Sqrt).then_inc(s_sd, 1)


@phase
def attention(nc, k, adj_d, qkv, out, identb):
    PIECE = 7
    NPC = NT // PIECE
    Q = 4
    quads = [(a, min(a + Q, NT)) for a in range(0, NT, Q)]
    NQD = len(quads)
    LOW, HIGH = float(np.exp(-5.0)), float(np.exp(5.0))

    def back(j):
        return j - 4 if j >= 4 else (NQD - 1 - (NQD - 1 - j) % 4) - NQD

    s_set, s_tr, s_qt = k.sem("at_set"), k.sem("at_turned"), k.sem("at_qt")
    s_in = [k.sem(f"at_in{j}") for j in range(2)]
    s_q, s_s, s_e, s_w, s_sum, s_out = (k.sem("at_" + n) for n in ("query", "score", "exp", "weight", "sum", "out"))
    with ExitStack() as own:
        src = k.sb("at_src", [P, 2, NT, P], BF16, own)
        ask = k.sb("at_ask", [P, NT, 3, P], BF16, own)
        v1 = k.sb("at_v1", [P, NT, D + 1], F32, own)
        with ExitStack() as prep:
            split = k.sb("at_split", [P, NT, 3, D], BF16, prep)
            stage = k.sb("at_stage", [P, 5, P], BF16, prep)
            turned = k.ps("at_turned", [P, 5, P], BF16, prep)
            block = prep.enter_context(nc.Block())

            @block.vector
            def _(dve):
                dve.memset(v1[:], 1.0)
                dve.drain()
                dve.tensor_copy(v1[:, :, 0:D], qkv[:, :, D:2 * D])
                split3(dve, qkv[:, :, 0:D], lambda j: split[:, :, j, :], out[:])
                halves = stage[:].rearrange("p c (b f) -> p (c b) f", b=2)
                dve.drain()
                with dve.Fori(0, NT) as t:
                    dve.tensor_copy(halves[:, 0:3, :], split[:, bass.ds(t, 1), :, :].rearrange("p t c f -> p (t c) f"))
                    dve.drain()
                    dve.tensor_copy(halves[:, 3:6, :], halves[:, 0:1, :].to_broadcast([P, 3, D]))
                    dve.tensor_copy(halves[:, 6:8, :], halves[:, 1:2, :].to_broadcast([P, 2, D]))
                    dve.tensor_copy(halves[:, 8, :], halves[:, 0, :])
                    dve.tensor_copy(halves[:, 9, :], halves[:, 2, :]).then_inc(s_set, 1)
                    dve.wait_ge(s_tr, t + 1)
                    dve.nop(nofuse=True)
                    dve.tensor_copy(src[:, :, bass.ds(t, 1), :].rearrange("p a t n -> p a (t n)"), turned[:, 0:2, :])
                    dve.tensor_copy(ask[:, bass.ds(t, 1), :, :].rearrange("p t c n -> p (t c) n"), turned[:, 2:5, :])
                    dve.drain()

            @block.tensor
            def _(pe):
                with pe.Fori(0, NT) as t:
                    pe.wait_ge(s_set, t + 1)
                    pe.nop(nofuse=True)
                    for j in range(5):
                        last = pe.transpose(turned[:, j, :], stage[:, j, :], identb[:])
                    last.then_inc(s_tr, 1)

        adj = k.sb("at_adj", [P, 2, NT * P], BF16, own)
        query = k.sb("at_query", [P, 2, 3, P], BF16, own)
        ex = k.sb("at_ex", [P, 4, Q * P], F32, own)
        wt = k.sb("at_wt", [P, 4, Q * P], F32, own)
        den = k.sb("at_den", [P, 2], F32, own)
        sps = [k.ps(f"at_s{j}", [P, 512], F32, own) for j in range(4)]
        ops = [k.ps(f"at_o{j}", [P, 512], F32, own) for j in range(2)]
        block = own.enter_context(nc.Block())

        @block.sync
        def _(sp):
            def tile(t, n, b):
                sp.wait_ge(s_out, t + 1)
                sp.dma_start(adj[:, b, :], adj_d[bass.ds(t, 1), :, :].rearrange("a p f -> (a p) f")).then_inc(s_in[b], 16)
            with sp.Fori(0, NT // 2) as i:
                for b in range(2):
                    tile(i * 2 + b, i, b)
            tile(NT - 1, NT // 2, 0)

        @block.tensor
        def _(pe):
            pe.sem_inc(s_sum, FREE)

            def tile(t, b):
                pe.wait_ge(s_q, t + 1)
                pe.wait_ge(s_out, t + 1)

                def total(j):
                    a, z = quads[j]
                    pe.wait_ge(s_w, t * NQD + (j + 1 + FREE))
                    for c in range(a, z):
                        last = pe.matmul(ops[b][:, 0:D + 1], wt[:, j % 4, (c - a) * P:(c - a + 1) * P], v1[:, c, :],
                                         start=(c == 0), stop=(c == NT - 1))
                    last.then_inc(s_sum, 1)

                for j, (a, z) in enumerate(quads):
                    pe.wait_ge(s_e, t * NQD + (back(j) + 1 + FREE))
                    for c in range(a, z):
                        to = sps[j % 4][:, (c - a) * P:(c - a + 1) * P]
                        pe.matmul(to, src[:, 1, c, :], query[:, b, 2, :], start=True, stop=False)
                        pe.matmul(to, src[:, 0, c, :], query[:, b, 1, :], start=False, stop=False)
                        last = pe.matmul(to, src[:, 0, c, :], query[:, b, 0, :], start=False, stop=True)
                    last.then_inc(s_s, 1)
                    if j >= 2:
                        total(j - 2)
                total(NQD - 2)
                total(NQD - 1)

            with pe.Fori(0, NT // 2) as i:
                for b in range(2):
                    tile(i * 2 + b, b)
            tile(NT - 1, 0)

        @block.scalar
        def _(act):
            act.sem_inc(s_e, FREE)

            def tile(t, b):
                for j, (a, z) in enumerate(quads):
                    act.wait_ge(s_s, t * NQD + (j + 1))
                    act.wait_ge(s_w, t * NQD + (back(j) + 1 + FREE))
                    act.activation(ex[:, j % 4, 0:(z - a) * P], sps[j % 4][:, 0:(z - a) * P], ACT.Exp,
                                   scale=1.0 / 8.0).then_inc(s_e, 1)

            with act.Fori(0, NT // 2) as i:
                for b in range(2):
                    tile(i * 2 + b, b)
            tile(NT - 1, 0)

        @block.vector
        def _(dve):
            dve.sem_inc(s_w, FREE)
            dve.sem_inc(s_out, 2)
            dve.tensor_copy(query[:, 0, :, :], ask[:, 0, :, :]).then_inc(s_q, 1)

            def tile(t, n, b, more):
                if more:
                    dve.tensor_copy(query[:, 1 - b, :, :], ask[:, bass.ds(t + 1, 1), :, :].rearrange("p a c n -> p (a c) n")).then_inc(s_q, 1)
                dve.wait_ge(s_in[b], n * 16 + 16)
                for j, (a, z) in enumerate(quads):
                    w = (z - a) * P
                    e = ex[:, j % 4, 0:w]
                    dve.wait_ge(s_e, t * NQD + (j + 1 + FREE))
                    dve.tensor_scalar(e, e, HIGH, LOW, ALU.min, ALU.max)
                    dve.drain()
                    dve.wait_ge(s_sum, t * NQD + (back(j) + 1 + FREE))
                    dve.tensor_tensor(wt[:, j % 4, 0:w], e, adj[:, b, a * P:z * P], ALU.mult).then_inc(s_w, 1)
                dve.wait_ge(s_sum, t * NQD + (NQD + FREE))
                dve.tensor_scalar(den[:, 0:1], ops[b][:, D:D + 1], 1e-30, None, ALU.max)
                dve.drain()
                dve.reciprocal(den[:, 1:2], den[:, 0:1])
                dve.drain()
                dve.tensor_scalar(out[:, bass.ds(t, 1), :].rearrange("p a f -> p (a f)"), ops[b][:, 0:D], den[:, 1:2],
                                  None, ALU.mult).then_inc(s_out, 1)

            with dve.Fori(0, NT // 2) as i:
                for b in range(2):
                    tile(i * 2 + b, i, b, True)
            tile(NT - 1, NT // 2, 0, False)


def add_wide(nc, k, x, y, scale=None, shift=None, relu=False):
    with nc.Block() as block:
        @block.vector
        def _(dve):
            if scale is not None:
                dve.tensor_tensor(y[:], y[:], scale[:].unsqueeze(1).to_broadcast([P, NT, D]), ALU.mult)
                dve.drain()
                dve.tensor_tensor(y[:], y[:], shift[:].unsqueeze(1).to_broadcast([P, NT, D]), ALU.add)
                dve.drain()
            dve.tensor_tensor(x[:], x[:], y[:], ALU.add)


def gin_input(nc, k, z, h, eps_sb):
    with nc.Block() as block:
        @block.vector
        def _(dve):
            dve.tensor_scalar(eps_sb[:], eps_sb[:], 1.0, None, ALU.add)
            dve.drain()
            dve.scalar_tensor_tensor(z[:], h[:], eps_sb[:, 0:1], z[:], ALU.mult, ALU.add)


@phase
def degree_scale(nc, k, deg, dinv):
    s_d, s_r = k.sem("deg_plus"), k.sem("deg_root")
    with nc.Block() as block:
        @block.vector
        def _(dve):
            dve.tensor_scalar(deg[:, 0:NT], deg[:, 0:NT], 1.0, None, ALU.add).then_inc(s_d, 1)
            dve.wait_ge(s_r, 1)
            dve.reciprocal(dinv[:, 0:NT], dinv[:, 0:NT])

        @block.scalar
        def _(act):
            act.wait_ge(s_d, 1)
            act.activation(dinv[:, 0:NT], deg[:, 0:NT], ACT.Sqrt).then_inc(s_r, 1)


def gcn_output(nc, k, z, y, dinv, bias=None, x=None):
    with nc.Block() as block:
        @block.vector
        def _(dve):
            dve.tensor_tensor(z[:], z[:], y[:], ALU.add)
            dve.drain()
            dve.tensor_tensor(z[:], z[:], per_node(dinv), ALU.mult)
            if bias is not None:
                dve.drain()
                dve.tensor_tensor(z[:], z[:], bias[:].unsqueeze(1).to_broadcast([P, NT, D]), ALU.add)
                dve.drain()
                dve.tensor_tensor(x[:], x[:], z[:], ALU.add)


STAGE = "full"


def build(nc, ins, out_d, stage):
    ctx = ExitStack()
    with ctx:
        k = Kit(nc, ctx)
        dram = lambda n, s, d: nc.dram_tensor(n, s, d).ap()
        rows_d = dram("rows_scr", (NP, ROW), F32)
        dst16_d = dram("dst16_scr", (EP,), I16)
        code_d = dram("code_scr", (LEAD + VTAB,), I32)
        scr_d = dram("table_scr", (2 * NGP,), F32)
        mm_d = dram("chunk_scr", (2 * NCC * P,), F32)
        wt_d = dram("window_scr", (NWP,), I32)
        adj_d = dram("adj_scr", (NT, P, NT * P), BF16)
        node = lambda n, c, w=D, d=F32: k.sb(n, [P, NT, w], d, c)
        x = node("x_sb", ctx)
        h = node("h_sb", ctx)
        ident = k.sb("ident", [P, P])
        ones = k.sb("ones", [P, P])
        identb = k.sb("identb", [P, P], BF16)
        iota_node = k.sb("iota_node", [P, NT + 1])
        turns = k.sb("turns", [P, 1], I32)
        stats = k.sb("stats", [P, 4, NT + 1])
        vec = {n: k.sb("v_" + n, [P, D]) for n in ("bo1", "bo2", "ln_g", "ln_b", "gcn_b2")}
        eps_sb = k.sb("v_eps", [P, 1])
        load_nodes(nc, k, ins["x"], x, ident, identb, iota_node, ones)
        load_vectors(nc, k, ins, vec, eps_sb)
        visit_list(nc, k, ins["dst_row"], dst16_d, code_d, turns, scr_d, ident)
        adjacency(nc, k, ins["dst_row"], ins["src_c"], ins["dst_c"], adj_d, mm_d, wt_d)

        def norm(tag, src, dst, **kw):
            with ExitStack() as own:
                layer_norm(nc, k, tag, src, dst, node(tag + "_tmp", own), stats, **kw)

        norm("ln0", x, h, relu_out=True)
        with ExitStack() as lay:
            g = node("g_sb", lay)
            for n in (1, 2):
                tag = f"gat{n}"
                with ExitStack() as edges:
                    xr3 = k.sb(tag + "_xr3", [P, NT + 1, 3, D], BF16, edges)
                    with ExitStack() as own:
                        xlr = node(tag + "_xlr", own, 2 * D)
                        linear(nc, k, tag + "_lin", h if n == 1 else g, ins[f"wlr{n}"], 2 * D, xlr, ident)
                        gat_tables(nc, k, tag + "_tab", xlr, xr3, rows_d)
                    acc = k.sb(tag + "_acc", [P, NT + 1, D + 1], F32, edges)
                    gat_edges(nc, k, tag, ins["ea"], ins["src_g"], dst16_d.rearrange("(g e) -> g e", e=GE), code_d,
                              rows_d, ins[f"we{n}"], ins[f"att{n}"], xr3, acc, ident, identb, iota_node, turns)
                    if n == 1:
                        gat_mean(nc, k, acc, g, vec["bo1"], stats)
                    else:
                        with ExitStack() as own:
                            skip = node("skip", own)
                            linear(nc, k, "skip", h, ins["wskip"], D, skip, ident)
                            gat_mean(nc, k, acc, g, vec["bo2"], stats, skip)
                if n == 1:
                    if stage == "gat1":
                        return store_nodes(nc, k, g, out_d)
                    norm("in1", g, g, relu_in=True)
                else:
                    norm("in2", g, g, relu_in=True, add_to=x)
        if stage == "L0":
            return store_nodes(nc, k, x, out_d)

        norm("ln1", x, h, relu_out=True)
        parts = node("parts", ctx, 3 * D + 1, BF16)
        z = node("z_sb", ctx)
        deg = k.sb("deg", [P, NT + 1])
        dinv = k.sb("dinv", [P, NT + 1])
        to_parts(nc, k, "gin", h, parts)
        propagate(nc, k, "gin_sum", adj_d, parts, z, deg)
        gin_input(nc, k, z, h, eps_sb)
        mlp(nc, k, "gin_mlp", z, ins["gin_w1"], D, ins["gin_w2"], 1, z, ident)
        batch_norm(nc, k, z, h, x, ones, ins["gin_gb"])
        if stage == "L1":
            return store_nodes(nc, k, x, out_d)

        norm("ln2", x, h, relu_out=True)
        with ExitStack() as own:
            qkv = node("qkv", own, 2 * D)
            linear(nc, k, "qkv_lin", h, ins["w_qkv"], 2 * D, qkv, ident)
            attention(nc, k, adj_d, qkv, z, identb)
            linear(nc, k, "o_lin", z, ins["w_o"], D, qkv, ident)
            add_pair(nc, k, z, qkv, h)
        norm("at_ln", z, z)
        add_wide(nc, k, x, z, vec["ln_g"], vec["ln_b"])
        if stage == "L2":
            return store_nodes(nc, k, x, out_d)

        norm("ln3", x, h, relu_out=True)
        degree_scale(nc, k, deg, dinv)
        to_parts(nc, k, "gcn1", h, parts, scale=dinv)
        propagate(nc, k, "gcn1_sum", adj_d, parts, z, None)
        gcn_output(nc, k, z, h, dinv)
        mlp(nc, k, "gcn_mlp", z, ins["gcn_w1"], P, ins["gcn_w2"], 0, h, ident)
        to_parts(nc, k, "gcn2", h, parts, scale=dinv)
        propagate(nc, k, "gcn2_sum", adj_d, parts, z, None)
        gcn_output(nc, k, z, h, dinv, vec["gcn_b2"], x)
        store_nodes(nc, k, x, out_d)


def add_pair(nc, k, out, a, h):
    with nc.Block() as block:
        @block.vector
        def _(dve):
            dve.tensor_tensor(out[:], a[:, :, 0:D], h[:], ALU.add)


@phase
def load_vectors(nc, k, ins, vec, eps_sb):
    s = k.sem("vectors_in")
    with nc.Block() as block:
        @block.sync
        def _(sp):
            for n, v in vec.items():
                sp.dma_start(v[:], ins[n].to_broadcast([P, D])).then_inc(s, 16)
            sp.dma_start(eps_sb[:], ins["eps"].to_broadcast([P, 1])).then_inc(s, 16)
            sp.wait_ge(s, 16 * (len(vec) + 1))


@phase
def store_nodes(nc, k, x, out_d):
    s = k.sem("stored")
    full = N // P
    with nc.Block() as block:
        @block.sync
        def _(sp):
            sp.dma_start(out_d[0:full * P, :].rearrange("(t p) f -> p t f", p=P), x[:, 0:full, :]).then_inc(s, 16)
            sp.dma_start(out_d[full * P:N, :], x[0:N - full * P, full, :]).then_inc(s, 16)
            sp.wait_ge(s, 32)


def lay_out(i):
    a = {n: np.asarray(v) for n, v in i.items()}
    pad = EP - E
    src = np.concatenate([a["src"].astype(np.int32, copy=False), np.zeros(pad, np.int32)])
    dst = np.concatenate([a["dst"].astype(np.int32, copy=False), np.full(pad, NP - 1, np.int32)])
    ea = np.concatenate([a["edge_attr_64"], np.zeros((pad, D), np.float32)])
    o = {"x": a["x"], "dst_row": dst}
    o["src_g"] = src.reshape(NG, GC, P).transpose(0, 2, 1)
    o["src_c"] = src.reshape(EP // P, P).T
    o["dst_c"] = dst.reshape(EP // P, P).T
    o["ea"] = ea.reshape(NG, 2, GE // 2, D).transpose(0, 1, 3, 2).reshape(NG, P, GE // 2)
    for n in (1, 2):
        w = lambda s: a[f"L0_gnn_{s}{n}"]
        o[f"wlr{n}"] = np.concatenate([np.concatenate([w("Wl").T, w("Wr").T], 1),
                                       np.concatenate([w("bl"), w("br")])[None]], 0)
        we = np.zeros((P, P), np.float32)
        we[:D, :D] = w("We").T
        we[D:, D:] = w("We").T
        o[f"we{n}"] = we
        att = np.zeros((2, D, 2, P), np.float32)
        att[0, :, 0] = att[1, :, 1] = w("att")[:, None]
        o[f"att{n}"] = att.reshape(P, 2, P)
        o[f"bo{n}"] = w("bo")[None]
    stack = lambda m, b: np.concatenate([m, b[None]], 0)
    o["wskip"] = stack(a["L0_gnn_Wskip"].T, a["L0_gnn_bskip"])
    o["gin_w1"] = stack(a["L1_gnn_W1"], a["L1_gnn_b1"])
    o["gin_w2"] = stack(a["L1_gnn_W2"], a["L1_gnn_b2"])
    o["gin_gb"] = np.stack([a["L1_gnn_gamma"], a["L1_gnn_beta"]])
    o["eps"] = a["L1_gnn_eps"].reshape(1, 1)
    o["w_qkv"] = stack(np.concatenate([a["L2_gnn_qk_w"].T, a["L2_gnn_v_w"].T], 1),
                       np.concatenate([a["L2_gnn_qk_b"], a["L2_gnn_v_b"]]))
    o["w_o"] = stack(a["L2_gnn_o_w"].T, a["L2_gnn_o_b"])
    o["ln_g"] = a["L2_gnn_ln_g"][None]
    o["ln_b"] = a["L2_gnn_ln_b"][None]
    o["gcn_w1"] = stack(a["L3_gnn_W1"], a["L3_gnn_b1"])
    o["gcn_w2"] = a["L3_gnn_W2"]
    o["gcn_b2"] = a["L3_gnn_b2"][None]
    return {n: np.ascontiguousarray(v) for n, v in o.items()}


def kernel(**inputs):
    import concourse.bacc as _bacc
    from concourse.bass_utils import run_bass_kernel_spmd as _run

    nc = _bacc.Bacc("TRN2", target_bir_lowering=False, num_devices=1)
    arrays = lay_out(inputs)
    ins = {n: nc.dram_tensor(f"in_{n}", v.shape, mybir.dt.from_np(v.dtype), kind="ExternalInput").ap()
           for n, v in arrays.items()}
    out_d = nc.dram_tensor("out_x", (N, D), F32, kind="ExternalOutput").ap()
    build(nc, ins, out_d, STAGE)
    r = _run(nc, [{f"in_{n}": v for n, v in arrays.items()}], core_ids=[0])
    return r.results[0]["out_x"]
```
